# Optimizing a Trainium2 kernel written in Bass

```python
import numpy as np
import jax
import jax.numpy as jnp

def _softmax(x, axis=-1):
    return jax.nn.softmax(x, axis=axis)

def _gelu(x):
    return jax.nn.gelu(x, approximate=True)

def _silu(x):
    return jax.nn.silu(x)

def _sigmoid(x):
    return jax.nn.sigmoid(x)

def _layernorm(x, axis=-1, eps=1e-05):
    m = jnp.mean(x, axis=axis, keepdims=True)
    v = jnp.var(x, axis=axis, keepdims=True)
    return (x - m) / jnp.sqrt(v + eps)

def _scatter_add(tgt, idx, src, axis=0):
    return tgt.at[idx].add(src)

def _segment_sum(src, seg, n):
    return jax.ops.segment_sum(src, seg, n)
kernel_name = 'mk_dlrm_tower_d1_rec_r8_bbb537'

def setup_inputs(seed: int=0):
    np.random.seed(seed)
    _w = jnp.asarray

    def _rec_inputs():
        import jax
        import jax.numpy as jnp
        _tk = jax.random.key(seed)
        dense_ctx = jax.random.normal(jax.random.fold_in(_tk, 190), (2048, 16), jnp.float32)
        ids = jnp.stack([jax.random.randint(jax.random.fold_in(_tk, 200 + f), (2048,), 0, v, jnp.int32) for f, v in enumerate([1000, 12500, 125000, 1250, 1000, 1250, 1000, 1250, 1250, 12500, 12500, 12500, 1000, 12500, 1250, 12500, 12500, 1000, 1000, 1250, 12500, 1250, 1250, 1250, 1000, 1250, 1000])], axis=1)
        tbl_0 = 0.05 * jax.random.normal(jax.random.fold_in(_tk, 500 + 0), (1000, 128), jnp.float32)
        tbl_1 = 0.05 * jax.random.normal(jax.random.fold_in(_tk, 500 + 1), (12500, 128), jnp.float32)
        tbl_2 = 0.05 * jax.random.normal(jax.random.fold_in(_tk, 500 + 2), (125000, 128), jnp.float32)
        tbl_3 = 0.05 * jax.random.normal(jax.random.fold_in(_tk, 500 + 3), (1250, 128), jnp.float32)
        tbl_4 = 0.05 * jax.random.normal(jax.random.fold_in(_tk, 500 + 4), (1000, 128), jnp.float32)
        tbl_5 = 0.05 * jax.random.normal(jax.random.fold_in(_tk, 500 + 5), (1250, 128), jnp.float32)
        tbl_6 = 0.05 * jax.random.normal(jax.random.fold_in(_tk, 500 + 6), (1000, 128), jnp.float32)
        tbl_7 = 0.05 * jax.random.normal(jax.random.fold_in(_tk, 500 + 7), (1250, 128), jnp.float32)
        tbl_8 = 0.05 * jax.random.normal(jax.random.fold_in(_tk, 500 + 8), (1250, 128), jnp.float32)
        tbl_9 = 0.05 * jax.random.normal(jax.random.fold_in(_tk, 500 + 9), (12500, 128), jnp.float32)
        tbl_10 = 0.05 * jax.random.normal(jax.random.fold_in(_tk, 500 + 10), (12500, 128), jnp.float32)
        tbl_11 = 0.05 * jax.random.normal(jax.random.fold_in(_tk, 500 + 11), (12500, 128), jnp.float32)
        tbl_12 = 0.05 * jax.random.normal(jax.random.fold_in(_tk, 500 + 12), (1000, 128), jnp.float32)
        tbl_13 = 0.05 * jax.random.normal(jax.random.fold_in(_tk, 500 + 13), (12500, 128), jnp.float32)
        tbl_14 = 0.05 * jax.random.normal(jax.random.fold_in(_tk, 500 + 14), (1250, 128), jnp.float32)
        tbl_15 = 0.05 * jax.random.normal(jax.random.fold_in(_tk, 500 + 15), (12500, 128), jnp.float32)
        tbl_16 = 0.05 * jax.random.normal(jax.random.fold_in(_tk, 500 + 16), (12500, 128), jnp.float32)
        tbl_17 = 0.05 * jax.random.normal(jax.random.fold_in(_tk, 500 + 17), (1000, 128), jnp.float32)
        tbl_18 = 0.05 * jax.random.normal(jax.random.fold_in(_tk, 500 + 18), (1000, 128), jnp.float32)
        tbl_19 = 0.05 * jax.random.normal(jax.random.fold_in(_tk, 500 + 19), (1250, 128), jnp.float32)
        tbl_20 = 0.05 * jax.random.normal(jax.random.fold_in(_tk, 500 + 20), (12500, 128), jnp.float32)
        tbl_21 = 0.05 * jax.random.normal(jax.random.fold_in(_tk, 500 + 21), (1250, 128), jnp.float32)
        tbl_22 = 0.05 * jax.random.normal(jax.random.fold_in(_tk, 500 + 22), (1250, 128), jnp.float32)
        tbl_23 = 0.05 * jax.random.normal(jax.random.fold_in(_tk, 500 + 23), (1250, 128), jnp.float32)
        tbl_24 = 0.05 * jax.random.normal(jax.random.fold_in(_tk, 500 + 24), (1000, 128), jnp.float32)
        tbl_25 = 0.05 * jax.random.normal(jax.random.fold_in(_tk, 500 + 25), (1250, 128), jnp.float32)
        tbl_26 = 0.05 * jax.random.normal(jax.random.fold_in(_tk, 500 + 26), (1000, 128), jnp.float32)
        _rk = jax.random.fold_in(_tk, 7)
        W_top1 = 0.0521996 * jax.random.normal(jax.random.fold_in(_tk, 801), (367, 512), jnp.float32)
        W_top2 = 0.0441942 * jax.random.normal(jax.random.fold_in(_tk, 802), (512, 256), jnp.float32)
        W_top3 = 0.0625 * jax.random.normal(jax.random.fold_in(_tk, 803), (256, 1), jnp.float32)
        b_top1 = jnp.zeros((512,), jnp.float32)
        b_top2 = jnp.zeros((256,), jnp.float32)
        return (dense_ctx, ids, tbl_0, tbl_1, tbl_2, tbl_3, tbl_4, tbl_5, tbl_6, tbl_7, tbl_8, tbl_9, tbl_10, tbl_11, tbl_12, tbl_13, tbl_14, tbl_15, tbl_16, tbl_17, tbl_18, tbl_19, tbl_20, tbl_21, tbl_22, tbl_23, tbl_24, tbl_25, tbl_26, W_top1, b_top1, W_top2, b_top2, W_top3)
    dense_ctx, ids, tbl_0, tbl_1, tbl_2, tbl_3, tbl_4, tbl_5, tbl_6, tbl_7, tbl_8, tbl_9, tbl_10, tbl_11, tbl_12, tbl_13, tbl_14, tbl_15, tbl_16, tbl_17, tbl_18, tbl_19, tbl_20, tbl_21, tbl_22, tbl_23, tbl_24, tbl_25, tbl_26, W_top1, b_top1, W_top2, b_top2, W_top3 = _rec_inputs()

    def _L0_rec_setup():
        import jax, jax.numpy as jnp
        import numpy as np

        def _tri_indices(num_feas):
            return np.array([i * num_feas + j for j in range(1, num_feas) for i in range(j)], dtype=np.int32)
        key = jax.random.key(seed)
        batch, num_feas, embed_dim = (2048, 27, 128)
        inputs = jax.random.normal(key, (batch, num_feas, embed_dim), dtype=jnp.float32)
        return {'inputs': inputs, 'num_feas': num_feas}
    _L0_rec_all = _L0_rec_setup()
    _L0_rec_in = {k: v for k, v in _L0_rec_all.items() if k in ()}
    del _L0_rec_all
    return {'dense_ctx': dense_ctx, 'ids': ids, 'tbl_0': tbl_0, 'tbl_1': tbl_1, 'tbl_2': tbl_2, 'tbl_3': tbl_3, 'tbl_4': tbl_4, 'tbl_5': tbl_5, 'tbl_6': tbl_6, 'tbl_7': tbl_7, 'tbl_8': tbl_8, 'tbl_9': tbl_9, 'tbl_10': tbl_10, 'tbl_11': tbl_11, 'tbl_12': tbl_12, 'tbl_13': tbl_13, 'tbl_14': tbl_14, 'tbl_15': tbl_15, 'tbl_16': tbl_16, 'tbl_17': tbl_17, 'tbl_18': tbl_18, 'tbl_19': tbl_19, 'tbl_20': tbl_20, 'tbl_21': tbl_21, 'tbl_22': tbl_22, 'tbl_23': tbl_23, 'tbl_24': tbl_24, 'tbl_25': tbl_25, 'tbl_26': tbl_26, 'W_top1': W_top1, 'b_top1': b_top1, 'W_top2': W_top2, 'b_top2': b_top2, 'W_top3': W_top3}

def reference(dense_ctx, ids, tbl_0, tbl_1, tbl_2, tbl_3, tbl_4, tbl_5, tbl_6, tbl_7, tbl_8, tbl_9, tbl_10, tbl_11, tbl_12, tbl_13, tbl_14, tbl_15, tbl_16, tbl_17, tbl_18, tbl_19, tbl_20, tbl_21, tbl_22, tbl_23, tbl_24, tbl_25, tbl_26, W_top1, b_top1, W_top2, b_top2, W_top3):
    import jax
    import jax.numpy as jnp

    def _L0_rec_ref(inputs, num_feas):
        import jax, jax.numpy as jnp
        import numpy as np

        def _tri_indices(num_feas):
            return np.array([i * num_feas + j for j in range(1, num_feas) for i in range(j)], dtype=np.int32)
        dot = jnp.einsum('bnd,bmd->bnm', inputs, inputs)
        idx = jnp.asarray(_tri_indices(num_feas))
        flat = dot.reshape(inputs.shape[0], num_feas * num_feas)
        return flat[:, idx]
    e = jnp.stack([tbl_0[ids[:, 0]], tbl_1[ids[:, 1]], tbl_2[ids[:, 2]], tbl_3[ids[:, 3]], tbl_4[ids[:, 4]], tbl_5[ids[:, 5]], tbl_6[ids[:, 6]], tbl_7[ids[:, 7]], tbl_8[ids[:, 8]], tbl_9[ids[:, 9]], tbl_10[ids[:, 10]], tbl_11[ids[:, 11]], tbl_12[ids[:, 12]], tbl_13[ids[:, 13]], tbl_14[ids[:, 14]], tbl_15[ids[:, 15]], tbl_16[ids[:, 16]], tbl_17[ids[:, 17]], tbl_18[ids[:, 18]], tbl_19[ids[:, 19]], tbl_20[ids[:, 20]], tbl_21[ids[:, 21]], tbl_22[ids[:, 22]], tbl_23[ids[:, 23]], tbl_24[ids[:, 24]], tbl_25[ids[:, 25]], tbl_26[ids[:, 26]]], axis=1)
    z = _L0_rec_ref(e, 27)
    z = z.reshape(z.shape[0], -1)
    h = jnp.concatenate([z, dense_ctx], axis=1)
    h = jnp.maximum(h @ W_top1 + b_top1, 0.0)
    h = jnp.maximum(h @ W_top2 + b_top2, 0.0)
    y = h @ W_top3
    return y

_drawn_inputs = setup_inputs


def setup_inputs(seed=0):
    import zlib

    import numpy as np

    out = dict(_drawn_inputs(seed))
    spreads = {'b_top1': (0.0, 0.1), 'b_top2': (0.0, 0.1)}
    factors = {}
    for name, (base, spread) in spreads.items():
        noise = np.random.default_rng([zlib.crc32(name.encode()), seed]).standard_normal(out[name].shape)
        drawn = base * np.exp(spread * noise) if base else spread * noise
        out[name] = jnp.asarray(drawn.astype(out[name].dtype))
    for name, factor in factors.items():
        out[name] = (out[name] * factor).astype(out[name].dtype)
    return out
```

```python
import concourse.bass as bass
from concourse import mybir

F32 = mybir.dt.float32
ALU = mybir.AluOpType
ACT = mybir.ActivationFunctionType

P = 128
QUAD = 32
NF = 27
D = 128
BATCH = 2048
TILES = BATCH // P
PAIRS = TILES // 2
CTX = 16
H1, H2 = 512, 256
C1, C2 = H1 // P, H2 // P
TG = 4
NTG = -(-NF // TG)
SG = 4
RG = 8
ROUNDS = P // (SG * RG)
NJ = NF - 1
JS = 7


def features_of(g):
    return list(range(TG * g, min(TG * g + TG, NF)))


def build(nc, dense_ctx, ids, tables, W1, b1, W2, b2, W3, out):
    ids_tiles = ids.rearrange("(p t) f -> p t f", t=TILES)
    ctx_tiles = dense_ctx.rearrange("(p t) c -> p t c", t=TILES)

    from contextlib import ExitStack
    stack = ExitStack()
    with stack:
        def sb(name, shape, dt=F32):
            return stack.enter_context(nc.sbuf_tensor(name, shape, dt))

        def ps(name, shape):
            return stack.enter_context(nc.psum_tensor(name, shape, F32))

        def sem(name):
            return stack.enter_context(nc.semaphore(name))

        ids_sb = [sb(f"ids_{h}", [P, NF], mybir.dt.int32) for h in range(2)]
        ctx_sb = [sb(f"ctx_{h}", [P, CTX]) for h in range(2)]
        rows = [sb(f"rows_{h}", [P, NF, D]) for h in range(2)]
        embT = [sb(f"embT_{h}", [P, P, QUAD]) for h in range(2)]
        dots = sb("dots", [P, JS, 2 * P])
        w1_sb = sb("w1_sb", [P, JS, H1])
        w2_sb = sb("w2_sb", [P, C1, H2])
        w3_sb = sb("w3_sb", [P, C2])
        b1_sb = sb("b1_sb", [P, C1])
        b2_sb = sb("b2_sb", [P, C2])
        h1_sb = sb("h1_sb", [P, C1, 2 * P])
        h2_sb = sb("h2_sb", [P, C2, 2 * P])
        y_sb = sb("y_sb", [P, TILES])
        ident = sb("ident", [P, P])

        pT = [ps(f"pT_{n}", [P, TG, P]) for n in range(2)]
        pG = [ps(f"pG_{n}", [P, RG, P]) for n in range(2)]
        pM = [ps(f"pM_{n}", [P, 2, 2 * P]) for n in range(2)]
        pY = pM[0][:, 1, 0:2]

        consts_loaded = sem("consts_loaded")
        w1_zeroed = sem("w1_zeroed")
        ident_steps = sem("ident_steps")
        zeroed = sem("zeroed")
        ids_loaded = [sem(f"ids_loaded_{h}") for h in range(2)]
        ctx_loaded = [sem(f"ctx_loaded_{h}") for h in range(2)]
        arrived = [[sem(f"arrived_{h}_{g}") for g in range(NTG)] for h in range(2)]
        rows_free = sem("rows_free")
        tiles_begun = sem("tiles_begun")
        transposed = sem("transposed")
        embT_v = sem("embT_v")
        embT_s = sem("embT_s")
        ctx_copied = sem("ctx_copied")
        multiplied = sem("multiplied")
        dots_v = sem("dots_v")
        dots_s = sem("dots_s")
        h1_summed = sem("h1_summed")
        h1_v, h1_s = sem("h1_v"), sem("h1_s")
        h2_summed = sem("h2_summed")
        h2_v, h2_s = sem("h2_v"), sem("h2_s")
        y_summed = sem("y_summed")
        y_copied = sem("y_copied")
        stored = sem("stored")

        N_CONSTS = (NF - 1) + 1 + 4

        block = stack.enter_context(nc.Block())

        @block.sync
        def _(sp):
            def load_tile(h, i):
                sp.dma_start(ids_sb[h][:, :], ids_tiles[:, 2 * i + h, :]).then_inc(ids_loaded[h], 16)
                sp.dma_start(ctx_sb[h][:, :], ctx_tiles[:, 2 * i + h, :]).then_inc(ctx_loaded[h], 16)

            for h in range(2):
                load_tile(h, 0)
            sp.dma_start(w2_sb[:, :, :], W2.rearrange("(c p) n -> p c n", p=P)).then_inc(consts_loaded, 16)
            sp.dma_start(w3_sb[:, :], W3.rearrange("(c p) o -> p (c o)", p=P),
                         allow_slow_non_contiguous=True).then_inc(consts_loaded, 16)
            sp.dma_start(b1_sb[:, :], b1.rearrange("(c p) -> p c", p=P),
                         allow_slow_non_contiguous=True).then_inc(consts_loaded, 16)
            sp.dma_start(b2_sb[:, :], b2.rearrange("(c p) -> p c", p=P),
                         allow_slow_non_contiguous=True).then_inc(consts_loaded, 16)
            with sp.Fori(1, PAIRS) as i:
                for h in range(2):
                    sp.wait_ge(transposed, 2 * NTG * i + NTG * (h - 1))
                    load_tile(h, i)
            sp.wait_ge(y_copied, PAIRS + 1)
            sp.dma_start(out.rearrange("(p t) o -> p (t o)", t=TILES), y_sb[:, :]).then_inc(stored, 16)
            sp.wait_ge(stored, 16)

        @block.gpsimd
        def _(pool):
            def gather_pair(i, first):
                for h in range(2):
                    if not first:
                        pool.wait_ge(transposed, 2 * NTG * i + NTG * (h - 1))
                        pool.sem_inc(rows_free, 1)
                    pool.wait_ge(ids_loaded[h], 16 * i + 16)
                    pool.sem_inc(tiles_begun, 1)
                    for g in range(NTG):
                        for f in features_of(g):
                            pool.indirect_dma_start(
                                rows[h][:, f, :], None, tables[f],
                                bass.IndirectOffsetOnAxis(ids_sb[h][:, f:f + 1], 0),
                            ).then_inc(arrived[h][g], 16)

            pool.memset(ident[:, :], 0.0).then_inc(ident_steps, 1)
            pool.wait_ge(ident_steps, 1)
            pool.affine_select(out=ident[:, :], in_=ident[:, :], compare_op=ALU.not_equal, fill=1.0,
                               base=0, pattern=[[-1, P]], channel_multiplier=1).then_inc(ident_steps, 1)
            gather_pair(0, True)
            with pool.Fori(1, PAIRS) as i:
                gather_pair(i, False)

        @block.tensor
        def _(pe):
            def transpose_group(h, g, i, first=False):
                n = NTG * h + g
                pe.wait_ge(arrived[h][g], 16 * len(features_of(g)) * (i + 1))
                if n >= 2 or not first:
                    pe.wait_ge((embT_v, embT_s)[n % 2], NTG * i + n // 2)
                for k, f in enumerate(features_of(g)):
                    last = nc.tensor.transpose(pT[n % 2][:, k, :], rows[h][:, f, :], ident[:, :])
                if g == NTG - 1:
                    pe.wait_ge(ctx_loaded[h], 16 * i + 16)
                    last = nc.tensor.transpose(pT[n % 2][0:CTX, TG - 1, :], ctx_sb[h][:, :], ident[:, :])
                last.then_inc(transposed, 1)

            def multiply_round(h, k, i, first=False):
                if k == 0:
                    pe.wait_ge(embT_v, NTG * i + (4, 7)[h])
                    pe.wait_ge(embT_s, NTG * i + (3, 7)[h])
                if not (first and k < 2):
                    pe.wait_ge(dots_v, 2 * ROUNDS * i + ROUNDS * h + k - 1)
                    pe.wait_ge(dots_s, 2 * ROUNDS * i + ROUNDS * h + k - 1)
                for n in range(RG):
                    s = SG * (RG * k + n)
                    last = nc.tensor.matmul(
                        pG[k % 2][:, n, 0:SG * NJ],
                        embT[h][:, s:s + SG, :].rearrange("p s f -> p (s f)"),
                        embT[h][:, s:s + SG, 1:NF], start=True, stop=True)
                last.then_inc(multiplied, 1)

            def layer1(i):
                pe.wait_ge(dots_v, 2 * ROUNDS * (i + 1))
                pe.wait_ge(dots_s, 2 * ROUNDS * (i + 1))
                pe.wait_ge(ctx_copied, 2 * i + 2)
                pe.wait_ge(y_copied, i + 1)
                for c in range(C1):
                    for s in range(JS):
                        last = nc.tensor.matmul(pM[c // 2][:, c % 2, :], w1_sb[:, s, P * c:P * c + P], dots[:, s, :],
                                                start=(s == 0), stop=(s == JS - 1))
                    if c % 2:
                        last.then_inc(h1_summed, 1)

            def layer2(i):
                pe.wait_ge(h1_s, 2 * i + 2)
                pe.wait_ge(h1_v, 2 * i + 2)
                for c in range(C2):
                    for k in range(C1):
                        last = nc.tensor.matmul(pM[c][:, 0, :], w2_sb[:, k, P * c:P * c + P], h1_sb[:, k, :],
                                                start=(k == 0), stop=(k == C1 - 1))
                    last.then_inc(h2_summed, 1)

            def layer3(i):
                pe.wait_ge(h2_s, i + 1)
                pe.wait_ge(h2_v, i + 1)
                for h in range(2):
                    for k in range(C2):
                        last = nc.tensor.matmul(pY[:, h:h + 1], h2_sb[:, k, P * h:P * h + P],
                                                w3_sb[:, k:k + 1], start=(k == 0), stop=(k == C2 - 1))
                last.then_inc(y_summed, 1)

            pe.wait_ge(ident_steps, 2)
            for g in range(NTG):
                transpose_group(0, g, 0, first=True)
            pe.wait_ge(zeroed, 3)
            for g in range(NTG):
                transpose_group(1, g, 0, first=True)
                if g < ROUNDS:
                    multiply_round(0, g, 0, first=True)
            pe.wait_ge(consts_loaded, 16 * N_CONSTS)
            with pe.Fori(1, PAIRS) as i:
                for g in range(NTG):
                    if g == 5:
                        layer2(i - 1)
                    if g == 6:
                        layer3(i - 1)
                    transpose_group(0, g, i)
                    if g < ROUNDS:
                        multiply_round(1, g, i - 1)
                    if g == 4:
                        layer1(i - 1)
                for g in range(NTG):
                    transpose_group(1, g, i)
                    if g < ROUNDS:
                        multiply_round(0, g, i)
            for g in range(ROUNDS):
                multiply_round(1, g, PAIRS - 1)
            layer1(PAIRS - 1)
            layer2(PAIRS - 1)
            layer3(PAIRS - 1)

        def copy_dots(copy, h, k, quadrants, done):
            for q in quadrants:
                for r in range(4):
                    j0, j1 = max(JS * r, 1), min(JS * r + JS, NF)
                    s0 = P * h + SG * RG * k + q
                    last = copy(
                        dots[QUAD * r:QUAD * r + QUAD, j0 - JS * r:j1 - JS * r, s0:s0 + SG * RG - SG + 1:SG]
                        .rearrange("p j n -> p n j"),
                        pG[k % 2][QUAD * q:QUAD * q + QUAD, :, NJ * q + j0 - 1:NJ * q + j1 - 1])
            last.then_inc(done, 1)

        def embT_of(h, g):
            f = features_of(g)
            return embT[h][:, :, f[0]:f[-1] + 1].rearrange("p s f -> p f s")

        @block.vector
        def _(dve):
            def copy_group(h, g, i):
                n = NTG * h + g
                if n % 2 == 0:
                    dve.wait_ge(transposed, 2 * NTG * i + n + 1)
                    if g == NTG - 1:
                        nc.vector.tensor_copy(dots[0:CTX, 0, P * h:P * h + P], pT[0][0:CTX, TG - 1, :])\
                            .then_inc(ctx_copied, 1)
                    nc.vector.tensor_copy(embT_of(h, g), pT[0][:, 0:len(features_of(g)), :]).then_inc(embT_v, 1)

            def copy_round(h, k, i):
                dve.wait_ge(multiplied, 2 * ROUNDS * i + ROUNDS * h + k + 1)
                copy_dots(nc.vector.tensor_copy, h, k, (0, 1), dots_v)

            def relu1(i):
                dve.wait_ge(h1_summed, 2 * i + 2)
                for c in (2, 3):
                    nc.vector.tensor_scalar(h1_sb[:, c, :], pM[1][:, c % 2, :], b1_sb[:, c:c + 1], 0.0, ALU.add, ALU.max)\
                        .then_inc(h1_v, 1)

            def relu2(i):
                dve.wait_ge(h2_summed, C2 * i + 2)
                nc.vector.tensor_scalar(h2_sb[:, 1, :], pM[1][:, 0, :], b2_sb[:, 1:2], 0.0, ALU.add, ALU.max)\
                    .then_inc(h2_v, 1)

            def copy_y(i):
                dve.wait_ge(y_summed, i + 1)
                nc.vector.tensor_copy(y_sb[:, bass.ds(2 * i, 2)], pY).then_inc(y_copied, 1)

            nc.vector.memset(w1_sb[:, :, :], 0.0).then_inc(w1_zeroed, 1)
            nc.vector.memset(embT[0][:, :, NF:QUAD], 0.0).then_inc(zeroed, 1)
            nc.vector.memset(embT[1][:, :, NF:QUAD], 0.0).then_inc(zeroed, 1)
            nc.vector.memset(dots[:, :, :], 0.0).then_inc(zeroed, 1)
            nc.vector.memset(y_sb[:, :], 0.0).then_inc(y_copied, 1)
            dve.wait_ge(zeroed, 3)
            for g in range(NTG):
                copy_group(0, g, 0)
            for g in range(NTG):
                copy_group(1, g, 0)
                if g < ROUNDS:
                    copy_round(0, g, 0)
            dve.wait_ge(consts_loaded, 16 * N_CONSTS)
            with dve.Fori(1, PAIRS) as i:
                for g in range(NTG):
                    if g == 5:
                        relu2(i - 1)
                    if g == 6:
                        copy_y(i - 1)
                    copy_group(0, g, i)
                    if g < ROUNDS:
                        copy_round(1, g, i - 1)
                    if g == 4:
                        relu1(i - 1)
                for g in range(NTG):
                    copy_group(1, g, i)
                    if g < ROUNDS:
                        copy_round(0, g, i)
            for g in range(ROUNDS):
                copy_round(1, g, PAIRS - 1)
            relu1(PAIRS - 1)
            relu2(PAIRS - 1)
            copy_y(PAIRS - 1)

        @block.scalar
        def _(act):
            def copy_group(h, g, i):
                n = NTG * h + g
                if n % 2 == 1:
                    act.wait_ge(transposed, 2 * NTG * i + n + 1)
                    if g == NTG - 1:
                        nc.scalar.copy(dots[0:CTX, 0, P * h:P * h + P], pT[1][0:CTX, TG - 1, :]).then_inc(ctx_copied, 1)
                    nc.scalar.copy(embT_of(h, g), pT[1][:, 0:len(features_of(g)), :]).then_inc(embT_s, 1)

            def copy_round(h, k, i):
                act.wait_ge(multiplied, 2 * ROUNDS * i + ROUNDS * h + k + 1)
                copy_dots(nc.scalar.copy, h, k, (2, 3), dots_s)

            def relu1(i):
                act.wait_ge(h1_summed, 2 * i + 1)
                for c in (0, 1):
                    nc.scalar.activation(h1_sb[:, c, :], pM[0][:, c, :], ACT.Relu, bias=b1_sb[:, c:c + 1]).then_inc(h1_s, 1)

            def relu2(i):
                act.wait_ge(h2_summed, C2 * i + 1)
                nc.scalar.activation(h2_sb[:, 0, :], pM[0][:, 0, :], ACT.Relu, bias=b2_sb[:, 0:1]).then_inc(h2_s, 1)

            act.wait_ge(w1_zeroed, 1)
            for j in range(1, NF):
                r, s, first = j // JS, j % JS, j * (j - 1) // 2
                act.dma_start(w1_sb[QUAD * r:QUAD * r + j, s, :], W1[first:first + j, :]).then_inc(consts_loaded, 16)
            act.dma_start(w1_sb[0:CTX, 0, :], W1[NF * (NF - 1) // 2:, :]).then_inc(consts_loaded, 16)

            act.wait_ge(zeroed, 3)
            for g in range(NTG):
                copy_group(0, g, 0)
            for g in range(NTG):
                copy_group(1, g, 0)
                if g < ROUNDS:
                    copy_round(0, g, 0)
            act.wait_ge(consts_loaded, 16 * N_CONSTS)
            with act.Fori(1, PAIRS) as i:
                for g in range(NTG):
                    if g == 5:
                        relu2(i - 1)
                    copy_group(0, g, i)
                    if g < ROUNDS:
                        copy_round(1, g, i - 1)
                    if g == 4:
                        relu1(i - 1)
                for g in range(NTG):
                    copy_group(1, g, i)
                    if g < ROUNDS:
                        copy_round(0, g, i)
            for g in range(ROUNDS):
                copy_round(1, g, PAIRS - 1)
            relu1(PAIRS - 1)
            relu2(PAIRS - 1)


_TABLES = [f"tbl_{f}" for f in range(NF)]
_INS = ["dense_ctx", "ids", *_TABLES, "W_top1", "b_top1", "W_top2", "b_top2", "W_top3"]


def kernel(**inputs):
    import numpy as _np
    import concourse.bacc as _bacc
    from concourse import mybir as _mybir
    from concourse.bass_utils import run_bass_kernel_spmd as _run

    nc = _bacc.Bacc("TRN2", target_bir_lowering=False, num_devices=1)
    arrays, aps = {}, {}
    for name in _INS:
        a = _np.ascontiguousarray(inputs[name])
        arrays[f"in_{name}_dram"] = a
        aps[name] = nc.dram_tensor(f"in_{name}_dram", a.shape, _mybir.dt.from_np(a.dtype), kind="ExternalInput").ap()
    out = nc.dram_tensor("out_0_dram", (BATCH, 1), _mybir.dt.float32, kind="ExternalOutput").ap()
    build(nc, aps["dense_ctx"], aps["ids"], [aps[t] for t in _TABLES], aps["W_top1"], aps["b_top1"],
          aps["W_top2"], aps["b_top2"], aps["W_top3"], out)
    r = _run(nc, [arrays], core_ids=[0])
    return r.results[0]["out_0_dram"]
```

```python
import concourse.bass as bass
from concourse import mybir

F32 = mybir.dt.float32
F32R = mybir.dt.float32r
F16 = mybir.dt.float16
I32 = mybir.dt.int32
ALU = mybir.AluOpType
ACT = mybir.ActivationFunctionType

P = 128
QUAD = 32
NF = 27
D = 128
BATCH = 2048
TILES = BATCH // P
PAIRS = TILES // 2
CTX = 16
H1, H2 = 512, 256
C1, C2 = H1 // P, H2 // P
SG = 4
RG = 8
ROUNDS = P // (SG * RG)
NJ = NF - 1
PROWS = (SG - 1) * QUAD + NJ
JS = 7

PICKED = (17, 18, 26, 24, 0, 12)
NPICK = len(PICKED)
GATHERED = [f for f in range(NF) if f not in PICKED]
VOCAB = 1000
VP = 125
VC = VOCAB // VP
PARTS = 2
NHOT = 3
TG = 4
WITH_CTX = 3
SIZES = [TG, TG, TG, 1, TG, TG]
NTG = len(SIZES)
GROUPS = [GATHERED[sum(SIZES[:g]):sum(SIZES[:g + 1])] for g in range(NTG)]
assert sum(SIZES) == len(GATHERED) and SIZES[WITH_CTX] + 2 <= TG

FIRST_TILE = [("rows", 0), ("rows", 1), ("rows", 2), ("rows", 3), ("pick", 0), ("pick", 1),
              ("rows", 4), ("pick", 2), ("pick", 3), ("rows", 5), ("pick", 4), ("pick", 5)]
FIRST_OF_ALL = [("rows", 0), ("pick", 0), ("pick", 1), ("rows", 1), ("pick", 2), ("rows", 2),
                ("pick", 3), ("rows", 3), ("rows", 4), ("rows", 5), ("pick", 4), ("pick", 5)]
SECOND_TILE = [("rows", g) for g in range(NTG)]
BANKS = len(FIRST_TILE) + len(SECOND_TILE)
assert BANKS % 2 == 0
assert all(FIRST_OF_ALL.index(x) <= FIRST_TILE.index(x)
           for x in [("rows", NTG - 1)] + [("pick", k) for k in range(NPICK - NHOT, NPICK)])


def runs(features):
    out = []
    for k, f in enumerate(features):
        if out and out[-1][1] + out[-1][2] == f:
            out[-1] = (out[-1][0], out[-1][1], out[-1][2] + 1)
        else:
            out.append((k, f, 1))
    return out


def emb_count(i, h, kind, k):
    first = FIRST_OF_ALL if isinstance(i, int) and i == 0 else FIRST_TILE
    n = len(first) + SECOND_TILE.index((kind, k)) if h else first.index((kind, k))
    return BANKS * i + n + 1


def build(nc, dense_ctx, ids, tables, W1, b1, W2, b2, W3, out):
    ids_tiles = ids.rearrange("(p t) f -> p t f", t=TILES)
    ctx_tiles = dense_ctx.rearrange("(p t) c -> p t c", t=TILES)
    ids_rows = nc.dram_tensor("ids_rows", (NPICK, BATCH), F16, kind="Internal").ap()

    from contextlib import ExitStack
    stack = ExitStack()
    with stack:
        def sb(name, shape, dt=F32):
            return stack.enter_context(nc.sbuf_tensor(name, shape, dt))

        def ps(name, shape):
            return stack.enter_context(nc.psum_tensor(name, shape, F32))

        def sem(name):
            return stack.enter_context(nc.semaphore(name))

        ids_sb = [sb(f"ids_{h}", [P, NF], I32) for h in range(2)]
        ctx_sb = sb("ctx_sb", [P, 2, CTX])
        rows = [sb(f"rows_{h}", [P, len(GATHERED), D]) for h in range(2)]
        embT = sb("embT", [P, 2 * P, QUAD])
        dots = sb("dots", [P, JS, 2 * P])
        w1_sb = sb("w1_sb", [P, JS, H1])
        w2_sb = sb("w2_sb", [P, C1, H2])
        w3_sb = sb("w3_sb", [P, C2])
        b1_sb = sb("b1_sb", [P, C1])
        b2_sb = sb("b2_sb", [P, C2])
        h1_sb = sb("h1_sb", [P, C1, 2 * P])
        h2_sb = sb("h2_sb", [P, C2, 2 * P])
        y_sb = sb("y_sb", [P, TILES])
        ident = sb("ident", [P, P])
        ids_all = sb("ids_all", [P, TILES, NF], I32)
        ids_f32 = sb("ids_f32", [P, NPICK, TILES])
        ids_f16 = sb("ids_f16", [NPICK * TILES, P], F16)
        ids_bc = sb("ids_bc", [P, NPICK, BATCH], F16)
        row_of_i32 = sb("row_of_i32", [P, VC], I32)
        row_of = sb("row_of", [P, VC])
        stage = [sb(f"stage_{n}", [P, VC * D]) for n in range(2)]
        late_rows = rows[1][:, :, :].rearrange("p f d -> p (f d)")
        table_f32 = [stage[0][:, :], stage[1][:, :], late_rows[:, 0:VC * D], late_rows[:, VC * D:2 * VC * D],
                     stage[0][:, :], stage[1][:, :]]
        parts = sb("parts", [P, NPICK, PARTS, VC * D], F32R)
        hot = sb("hot", [P, NHOT, VC, 2 * P], F32R)

        pE = [ps(f"pE_{n}", [P, TG, P]) for n in range(2)]
        pG = [ps(f"pG_{n}", [P, RG, P]) for n in range(2)]
        pM = [ps(f"pM_{n}", [P, 2, 2 * P]) for n in range(2)]
        pY = pM[0][:, 1, 0:2]
        pI = pM[0][:, 0, 0:P]

        w_loaded = sem("w_loaded")
        ids_all_loaded = sem("ids_all_loaded")
        ids_cast = sem("ids_cast")
        ids_turned = sem("ids_turned")
        ids_f16_made = sem("ids_f16_made")
        ids_rows_stored = sem("ids_rows_stored")
        ids_bc_loaded = [sem(f"ids_bc_loaded_{n}") for n in range(2)]
        row_of_steps = sem("row_of_steps")
        table_loaded = [sem(f"table_loaded_{k}") for k in range(NPICK)]
        part_s = sem("part_s")
        part_v = sem("part_v")
        w1_zeroed = sem("w1_zeroed")
        ident_steps = sem("ident_steps")
        zeroed = sem("zeroed")
        ids_loaded = [sem(f"ids_loaded_{h}") for h in range(2)]
        ctx_loaded = sem("ctx_loaded")
        arrived = [[sem(f"arrived_{h}_{g}") for g in range(NTG)] for h in range(2)]
        rows_free = sem("rows_free")
        tiles_begun = sem("tiles_begun")
        hot_made = sem("hot_made")
        emb_ready = sem("emb_ready")
        emb_copied = sem("emb_copied")
        multiplied = sem("multiplied")
        dots_v = sem("dots_v")
        dots_s = sem("dots_s")
        h1_summed = sem("h1_summed")
        h1_v, h1_s = sem("h1_v"), sem("h1_s")
        h2_summed = sem("h2_summed")
        h2_v, h2_s = sem("h2_v"), sem("h2_s")
        y_summed = sem("y_summed")
        y_copied = sem("y_copied")
        stored = sem("stored")

        W_DMAS = (NF - 1) + 1 + 4

        block = stack.enter_context(nc.Block())

        @block.sync
        def _(sp):
            def load_ids(h, i):
                sp.dma_start(ids_sb[h][:, :], ids_tiles[:, 2 * i + h, :]).then_inc(ids_loaded[h], 16)

            def load_ctx(i):
                sp.dma_start(ctx_sb[:, :, :], ctx_tiles[:, bass.ds(2 * i, 2), :]).then_inc(ctx_loaded, 16)

            def load_table(k):
                sp.dma_start(table_f32[k][0:VP, :], tables[PICKED[k]].rearrange("(p c) d -> p (c d)", c=VC))\
                  .then_inc(table_loaded[k], 16)

            sp.dma_start(ids_all[:, :, :], ids_tiles).then_inc(ids_all_loaded, 16)
            load_ids(0, 0)
            for k in range(3):
                load_table(k)
            sp.wait_ge(ids_f16_made, 1)
            sp.dma_start(ids_rows.rearrange("f (t p) -> (f t) p", p=P), ids_f16[:, :]).then_inc(ids_rows_stored, 16)
            load_table(3)
            sp.wait_ge(ids_rows_stored, 16)
            for at, to in ((0, 2 * P), (2 * P, BATCH)):
                sp.dma_start(ids_bc[:, :, at:to], ids_rows[:, at:to].partition_broadcast(P))\
                  .then_inc(ids_bc_loaded[at > 0], 16)
            load_ids(1, 0)
            load_ctx(0)
            for k in range(4, NPICK):
                sp.wait_ge(part_v, k - 3)
                load_table(k)
            sp.wait_ge(w1_zeroed, 1)
            for j in range(1, NF):
                r, s, first = j // JS, j % JS, j * (j - 1) // 2
                sp.dma_start(w1_sb[QUAD * r:QUAD * r + j, s, :], W1[first:first + j, :]).then_inc(w_loaded, 16)
            sp.dma_start(w1_sb[0:CTX, 0, :], W1[NF * (NF - 1) // 2:, :]).then_inc(w_loaded, 16)
            sp.dma_start(w2_sb[:, :, :], W2.rearrange("(c p) n -> p c n", p=P)).then_inc(w_loaded, 16)
            sp.dma_start(w3_sb[:, :], W3.rearrange("(c p) o -> p (c o)", p=P),
                         allow_slow_non_contiguous=True).then_inc(w_loaded, 16)
            sp.dma_start(b1_sb[:, :], b1.rearrange("(c p) -> p c", p=P),
                         allow_slow_non_contiguous=True).then_inc(w_loaded, 16)
            sp.dma_start(b2_sb[:, :], b2.rearrange("(c p) -> p c", p=P),
                         allow_slow_non_contiguous=True).then_inc(w_loaded, 16)
            with sp.Fori(1, PAIRS) as i:
                for h in range(2):
                    sp.wait_ge(emb_ready, emb_count(i - 1, h, "rows", NTG - 1))
                    load_ids(h, i)
                load_ctx(i)
            sp.wait_ge(y_copied, PAIRS + 2)
            sp.dma_start(out.rearrange("(p t) o -> p (t o)", t=TILES), y_sb[:, :]).then_inc(stored, 16)
            sp.wait_ge(stored, 16)

        @block.gpsimd
        def _(pool):
            def gather_pair(i, first):
                for h in range(2):
                    if not first:
                        pool.wait_ge(emb_ready, emb_count(i - 1, h, "rows", NTG - 1))
                        pool.sem_inc(rows_free, 1)
                    if first and h == 1:
                        pool.wait_ge(part_v, 4)
                    pool.wait_ge(ids_loaded[h], 16 * i + 16)
                    pool.sem_inc(tiles_begun, 1)
                    for g in range(NTG):
                        for f in GROUPS[g]:
                            pool.indirect_dma_start(
                                rows[h][:, GATHERED.index(f), :], None, tables[f],
                                bass.IndirectOffsetOnAxis(ids_sb[h][:, f:f + 1], 0),
                            ).then_inc(arrived[h][g], 16)

            pool.memset(ident[:, :], 0.0).then_inc(ident_steps, 1)
            pool.iota(row_of_i32[:, :], [[1, VC]], base=0, channel_multiplier=VC).then_inc(row_of_steps, 1)
            pool.wait_ge(ident_steps, 1)
            pool.affine_select(out=ident[:, :], in_=ident[:, :], compare_op=ALU.not_equal, fill=1.0,
                               base=0, pattern=[[-1, P]], channel_multiplier=1).then_inc(ident_steps, 1)
            gather_pair(0, True)
            with pool.Fori(1, PAIRS) as i:
                gather_pair(i, False)

        @block.tensor
        def _(pe):
            def bank_free(n, i, first):
                if n >= 2 or not first:
                    pe.wait_ge(emb_copied, BANKS * i + n - 1)

            def transpose_group(h, g, n, i, first=False):
                pe.wait_ge(arrived[h][g], 16 * len(GROUPS[g]) * (i + 1))
                bank_free(n, i, first)
                for k, f in enumerate(GROUPS[g]):
                    last = nc.tensor.transpose(pE[n % 2][:, k, :], rows[h][:, GATHERED.index(f), :], ident[:, :])
                if g == WITH_CTX and h == 1:
                    pe.wait_ge(ctx_loaded, 16 * i + 16)
                    for k in range(2):
                        last = nc.tensor.transpose(pE[n % 2][0:CTX, TG - 2 + k, :], ctx_sb[:, k, :], ident[:, :])
                last.then_inc(emb_ready, 1)

            def pick(k, n, i, first=False):
                if first:
                    pe.wait_ge(part_v, k + 1)
                pe.wait_ge(hot_made, NPICK * i + k + 1)
                bank_free(n, i, first)
                for c in range(VC):
                    for part in range(PARTS):
                        last = nc.tensor.matmul(
                            pE[n % 2][:, 0:2, :].rearrange("p a b -> p (a b)"), parts[0:VP, k, part, D * c:D * c + D],
                            hot[0:VP, k % NHOT, c, :], start=(c + part == 0), stop=(c == VC - 1 and part == PARTS - 1))
                last.then_inc(emb_ready, 1)

            def multiply_round(h, k, i, first=False):
                if k == 0:
                    pe.wait_ge(emb_copied, BANKS * i + (len(FIRST_TILE), BANKS)[h])
                if not (first and k < 2):
                    pe.wait_ge(dots_v, 2 * ROUNDS * i + ROUNDS * h + k - 1)
                    pe.wait_ge(dots_s, 2 * ROUNDS * i + ROUNDS * h + k - 1)
                for n in range(RG):
                    s = P * h + SG * (RG * k + n)
                    last = nc.tensor.matmul(
                        pG[k % 2][0:PROWS, n, 0:SG * NJ],
                        embT[:, s:s + SG, :].rearrange("p s f -> p (s f)")[:, 0:PROWS],
                        embT[:, s:s + SG, 1:NF], start=True, stop=True)
                last.then_inc(multiplied, 1)

            def layer1(n, rounds, at=0, size=2 * P):
                pe.wait_ge(dots_v, rounds)
                pe.wait_ge(dots_s, rounds)
                pe.wait_ge(y_copied, n + 1)
                for c in range(C1):
                    for s in range(JS):
                        last = nc.tensor.matmul(pM[c // 2][:, c % 2, 0:size], w1_sb[:, s, P * c:P * c + P],
                                                dots[:, s, at:at + size], start=(s == 0), stop=(s == JS - 1))
                    if c % 2:
                        last.then_inc(h1_summed, 1)

            def layer2(n, size=2 * P):
                pe.wait_ge(h1_s, 2 * n + 2)
                pe.wait_ge(h1_v, 2 * n + 2)
                for c in range(C2):
                    for k in range(C1):
                        last = nc.tensor.matmul(pM[c][:, 0, 0:size], w2_sb[:, k, P * c:P * c + P], h1_sb[:, k, 0:size],
                                                start=(k == 0), stop=(k == C1 - 1))
                    last.then_inc(h2_summed, 1)

            def layer3(n, size=2 * P):
                pe.wait_ge(h2_s, n + 1)
                pe.wait_ge(h2_v, n + 1)
                for h in range(size // P):
                    for k in range(C2):
                        last = nc.tensor.matmul(pY[:, h:h + 1], h2_sb[:, k, P * h:P * h + P],
                                                w3_sb[:, k:k + 1], start=(k == 0), stop=(k == C2 - 1))
                last.then_inc(y_summed, 1)

            def first_tile(i, first):
                for n, (kind, k) in enumerate(FIRST_OF_ALL if first else FIRST_TILE):
                    if kind == "rows":
                        transpose_group(0, k, n, i, first)
                        if not first and k < ROUNDS:
                            multiply_round(1, k, i - 1)
                    else:
                        pick(k, n, i, first)

            def second_tile(i, first, last):
                for g in range(NTG):
                    transpose_group(1, g, len(FIRST_TILE) + g, i, first)
                    if g == 0 and not first:
                        layer1(i - 1, 2 * ROUNDS * i)
                    if 1 <= g < ROUNDS:
                        multiply_round(0, g - 1, i, first)
                    if g == 2 and not first:
                        layer2(i - 1)
                    if g == 3 and not first:
                        layer3(i - 1)
                    if g == (WITH_CTX if last else NTG - 1):
                        multiply_round(0, ROUNDS - 1, i, first)
                    if g == 4 and last:
                        layer1(i, 2 * ROUNDS * i + ROUNDS, 0, P)

            pe.wait_ge(ident_steps, 2)
            pe.wait_ge(ids_cast, 1)
            nc.tensor.transpose(pI[0:NPICK * TILES, :], ids_f32[:, :, :].rearrange("p f t -> p (f t)"), ident[:, :])\
                .then_inc(ids_turned, 1)
            first_tile(0, True)
            pe.wait_ge(zeroed, 2)
            second_tile(0, True, False)
            pe.wait_ge(w_loaded, 16 * W_DMAS)
            with pe.Fori(1, PAIRS - 1) as i:
                first_tile(i, False)
                second_tile(i, False, False)
            first_tile(PAIRS - 1, False)
            second_tile(PAIRS - 1, False, True)
            layer2(PAIRS - 1, P)
            multiply_round(1, 0, PAIRS - 1)
            multiply_round(1, 1, PAIRS - 1)
            layer3(PAIRS - 1, P)
            multiply_round(1, 2, PAIRS - 1)
            multiply_round(1, 3, PAIRS - 1)
            layer1(PAIRS, 2 * ROUNDS * PAIRS, P, P)
            layer2(PAIRS, P)
            layer3(PAIRS, P)

        def copy_dots(copy, h, k, quadrants, done):
            for q in quadrants:
                n = min(QUAD, PROWS - QUAD * q)
                for r in range(4):
                    j0, j1 = max(JS * r, 1), min(JS * r + JS, NF)
                    s0 = P * h + SG * RG * k + q
                    last = copy(
                        dots[QUAD * r:QUAD * r + n, j0 - JS * r:j1 - JS * r, s0:s0 + SG * RG - SG + 1:SG]
                        .rearrange("p j n -> p n j"),
                        pG[k % 2][QUAD * q:QUAD * q + n, :, NJ * q + j0 - 1:NJ * q + j1 - 1])
            last.then_inc(done, 1)

        def copy_embeddings(copy, bank, h, kind, k):
            if kind == "pick":
                f = PICKED[k]
                last = copy(embT[:, :, f], bank[:, 0:2, :].rearrange("p a b -> p (a b)"))
            else:
                if h == 1 and k == WITH_CTX:
                    copy(dots[0:CTX, 0, :], bank[0:CTX, TG - 2:TG, :].rearrange("p a b -> p (a b)"))
                for at, f, count in runs(GROUPS[k]):
                    last = copy(embT[:, P * h:P * h + P, f:f + count].rearrange("p s f -> p f s"),
                                bank[:, at:at + count, :])
            last.then_inc(emb_copied, 1)

        @block.vector
        def _(dve):
            def make_hot(k, i, first):
                if k >= NHOT:
                    dve.wait_ge(emb_ready, emb_count(i, 0, "pick", k - NHOT))
                elif not first:
                    dve.wait_ge(emb_ready, emb_count(i - 1, 0, "pick", k + NHOT * ((NPICK - 1 - k) // NHOT)))
                for c in range(VC):
                    last = nc.vector.tensor_scalar(hot[0:VP, k % NHOT, c, :], ids_bc[0:VP, k, bass.ds(2 * P * i, 2 * P)],
                                                   row_of[0:VP, c:c + 1], None, ALU.is_equal)
                last.then_inc(hot_made, 1)

            def copy_round(h, k, i):
                dve.wait_ge(multiplied, 2 * ROUNDS * i + ROUNDS * h + k + 1)
                copy_dots(nc.vector.tensor_copy, h, k, (0, 1), dots_v)

            def relu1(n, size=2 * P):
                dve.wait_ge(h1_summed, 2 * n + 2)
                for c in (2, 3):
                    nc.vector.tensor_scalar(h1_sb[:, c, 0:size], pM[1][:, c % 2, 0:size], b1_sb[:, c:c + 1], 0.0,
                                            ALU.add, ALU.max).then_inc(h1_v, 1)

            def relu2(n, size=2 * P):
                dve.wait_ge(h2_summed, C2 * n + 2)
                nc.vector.tensor_scalar(h2_sb[:, 1, 0:size], pM[1][:, 0, 0:size], b2_sb[:, 1:2], 0.0,
                                        ALU.add, ALU.max).then_inc(h2_v, 1)

            def copy_y(n, at, size=2):
                dve.wait_ge(y_summed, n + 1)
                nc.vector.tensor_copy(y_sb[:, bass.ds(at, size)], pY[:, 0:size]).then_inc(y_copied, 1)

            def first_tile(i):
                for r in range(ROUNDS):
                    copy_round(1, r, i - 1)
                for k in range(NHOT, NPICK):
                    make_hot(k, i, False)

            def second_tile(i, last):
                if not last:
                    make_hot(0, i + 1, False)
                relu1(i - 1)
                copy_round(0, 0, i)
                copy_round(0, 1, i)
                if not last:
                    make_hot(1, i + 1, False)
                relu2(i - 1)
                copy_round(0, 2, i)
                copy_y(i - 1, 2 * (i - 1))
                if not last:
                    make_hot(2, i + 1, False)
                copy_round(0, 3, i)

            def second_part(k):
                dve.wait_ge(part_s, k + 1)
                nc.vector.tensor_tensor(parts[0:VP, k, 1, :], table_f32[k][0:VP, :], parts[0:VP, k, 0, :],
                                        ALU.subtract).then_inc(part_v, 1)

            nc.vector.memset(w1_sb[:, :, :], 0.0).then_inc(w1_zeroed, 1)
            dve.wait_ge(ids_all_loaded, 16)
            for k, f in enumerate(PICKED):
                last = nc.vector.tensor_copy(ids_f32[:, k, :], ids_all[:, :, f])
            last.then_inc(ids_cast, 1)
            dve.wait_ge(row_of_steps, 1)
            nc.vector.tensor_copy(row_of[:, :], row_of_i32[:, :]).then_inc(row_of_steps, 1)
            for k in range(4):
                second_part(k)
            dve.wait_ge(row_of_steps, 2)
            dve.wait_ge(ids_bc_loaded[0], 16)
            make_hot(0, 0, True)
            make_hot(1, 0, True)
            second_part(4)
            second_part(5)
            make_hot(2, 0, True)
            nc.vector.memset(embT[:, :, NF:QUAD], 0.0).then_inc(zeroed, 1)
            make_hot(3, 0, True)
            nc.vector.memset(dots[:, :, :], 0.0).then_inc(zeroed, 1)
            for k in range(4, NPICK):
                make_hot(k, 0, True)
            nc.vector.memset(y_sb[:, :], 0.0).then_inc(y_copied, 1)
            dve.wait_ge(zeroed, 2)
            dve.wait_ge(ids_bc_loaded[1], 16)
            for r in range(ROUNDS):
                copy_round(0, r, 0)
                if r < NHOT:
                    make_hot(r, 1, False)
            dve.wait_ge(w_loaded, 16 * W_DMAS)
            with dve.Fori(1, PAIRS - 1) as i:
                first_tile(i)
                second_tile(i, False)
            first_tile(PAIRS - 1)
            second_tile(PAIRS - 1, True)
            relu1(PAIRS - 1, P)
            relu2(PAIRS - 1, P)
            copy_round(1, 0, PAIRS - 1)
            copy_round(1, 1, PAIRS - 1)
            copy_y(PAIRS - 1, TILES - 2, 1)
            copy_round(1, 2, PAIRS - 1)
            copy_round(1, 3, PAIRS - 1)
            relu1(PAIRS, P)
            relu2(PAIRS, P)
            copy_y(PAIRS, TILES - 1, 1)

        @block.scalar
        def _(act):
            def copy_bank(h, n, kind, k, i):
                act.wait_ge(emb_ready, BANKS * i + n + 1)
                copy_embeddings(nc.scalar.copy, pE[n % 2], h, kind, k)

            def copy_round(h, k, i):
                act.wait_ge(multiplied, 2 * ROUNDS * i + ROUNDS * h + k + 1)
                copy_dots(nc.scalar.copy, h, k, (2, 3), dots_s)

            def relu1(n, size=2 * P):
                act.wait_ge(h1_summed, 2 * n + 1)
                for c in (0, 1):
                    nc.scalar.activation(h1_sb[:, c, 0:size], pM[0][:, c, 0:size], ACT.Relu, bias=b1_sb[:, c:c + 1])\
                        .then_inc(h1_s, 1)

            def relu2(n, size=2 * P):
                act.wait_ge(h2_summed, C2 * n + 1)
                nc.scalar.activation(h2_sb[:, 0, 0:size], pM[0][:, 0, 0:size], ACT.Relu, bias=b2_sb[:, 0:1])\
                    .then_inc(h2_s, 1)

            def first_tile(i, first):
                for n, (kind, k) in enumerate(FIRST_OF_ALL if first else FIRST_TILE):
                    copy_bank(0, n, kind, k, i)
                    if kind == "rows" and not first and k < ROUNDS:
                        copy_round(1, k, i - 1)

            def second_tile(i, first, last):
                for g in range(NTG):
                    copy_bank(1, len(FIRST_TILE) + g, "rows", g, i)
                    if g == 0 and not first:
                        relu1(i - 1)
                    if 1 <= g < ROUNDS:
                        copy_round(0, g - 1, i)
                    if g == 2 and not first:
                        relu2(i - 1)
                    if g == (WITH_CTX if last else NTG - 1):
                        copy_round(0, ROUNDS - 1, i)
                    if g == 4 and last:
                        relu1(i, P)

            act.wait_ge(ids_turned, 1)
            nc.scalar.copy(ids_f16[:, :], pI[0:NPICK * TILES, :]).then_inc(ids_f16_made, 1)
            for k in range(NPICK):
                act.wait_ge(table_loaded[k], 16)
                nc.scalar.copy(parts[0:VP, k, 0, :], table_f32[k][0:VP, :]).then_inc(part_s, 1)
            first_tile(0, True)
            act.wait_ge(zeroed, 2)
            second_tile(0, True, False)
            act.wait_ge(w_loaded, 16 * W_DMAS)
            with act.Fori(1, PAIRS - 1) as i:
                first_tile(i, False)
                second_tile(i, False, False)
            first_tile(PAIRS - 1, False)
            second_tile(PAIRS - 1, False, True)
            relu2(PAIRS - 1, P)
            for r in range(ROUNDS):
                copy_round(1, r, PAIRS - 1)
            relu1(PAIRS, P)
            relu2(PAIRS, P)


_TABLES = [f"tbl_{f}" for f in range(NF)]
_INS = ["dense_ctx", "ids", *_TABLES, "W_top1", "b_top1", "W_top2", "b_top2", "W_top3"]


def kernel(**inputs):
    import numpy as _np
    import concourse.bacc as _bacc
    from concourse import mybir as _mybir
    from concourse.bass_utils import run_bass_kernel_spmd as _run

    nc = _bacc.Bacc("TRN2", target_bir_lowering=False, num_devices=1)
    arrays, aps = {}, {}
    for name in _INS:
        a = _np.ascontiguousarray(inputs[name])
        arrays[f"in_{name}_dram"] = a
        aps[name] = nc.dram_tensor(f"in_{name}_dram", a.shape, _mybir.dt.from_np(a.dtype), kind="ExternalInput").ap()
    out = nc.dram_tensor("out_0_dram", (BATCH, 1), _mybir.dt.float32, kind="ExternalOutput").ap()
    build(nc, aps["dense_ctx"], aps["ids"], [aps[t] for t in _TABLES], aps["W_top1"], aps["b_top1"],
          aps["W_top2"], aps["b_top2"], aps["W_top3"], out)
    r = _run(nc, [arrays], core_ids=[0])
    return r.results[0]["out_0_dram"]
```

```python
import concourse.bass as bass
from concourse import mybir

F32 = mybir.dt.float32
F32R = mybir.dt.float32r
F16 = mybir.dt.float16
I32 = mybir.dt.int32
ALU = mybir.AluOpType
ACT = mybir.ActivationFunctionType

P = 128
QUAD = 32
NF = 27
D = 128
BATCH = 2048
TILES = BATCH // P
PAIRS = TILES // 2
CTX = 16
H1, H2 = 512, 256
C1, C2 = H1 // P, H2 // P
SG = 4
RG = 8
ROUNDS = P // (SG * RG)
HUBS = 3
X, Y, Z = HUBS, HUBS + (NF - HUBS) // 3, HUBS + 2 * (NF - HUBS) // 3
PLACES = NF + HUBS
NJ = NF - 1
PROWS = (SG - 1) * QUAD + PLACES
JS = 4
CTX_BLOCK = 4 * JS - 1
CTX_ROW = QUAD * (CTX_BLOCK // JS)

PACKING = [[(PLACES, 0, Z + 6, 4), (PLACES, 4, X + 4, 4), (PLACES, 8, Z, 4), (PLACES, 12, Z + 4, 3)],
           [(NF, 0, X, 4), (Z, 4, Y + 4, 3), (Z, 7, Z + 7, 1), (Y, 8, X, 4), (Y, 12, X + 4, 3)],
           [(Z, 0, Y, 4), (Y, 7, Y + 7, 1)]]
STEPS = len(PACKING)

PICKED = (17, 18, 26, 24, 0, 12, 6)
NPICK = len(PICKED)
GATHERED = [f for f in range(NF) if f not in PICKED]
VOCAB = 1000
VP = 125
VC = VOCAB // VP
PARTS = 2
NHOT = 3
TG = 4
NTG = len(GATHERED) // TG
assert NTG * TG == len(GATHERED)
GROUPS = [GATHERED[TG * g:TG * g + TG] for g in range(NTG)]

MORE = PICKED[-3:]

FIRST_TILE = [*(("rows", g) for g in range(ROUNDS)), *(("pick", k) for k in range(NPICK)), ("rows", NTG - 1)]
FIRST_OF_ALL = [("rows", 0), ("pick", 0), ("rows", 1), ("pick", 1), ("rows", 2), ("pick", 2), ("rows", 3),
                *(("pick", k) for k in range(3, NPICK)), ("rows", NTG - 1)]
SECOND_TILE = [("rows", 0), ("contexts", 0), *(("rows", g) for g in range(1, NTG))]
FIRST_OF_LAST = [*(x for x in FIRST_TILE if x[0] == "rows" or x[1] < NPICK - len(MORE)), ("more", 0)]
SECOND_OF_LAST = [("more", 0), *SECOND_TILE]
BANKS = len(FIRST_TILE) + len(SECOND_TILE)
assert BANKS % 2 == 0 and len(MORE) <= min(TG, NPICK - NHOT)
assert all(FIRST_OF_ALL.index(x) <= FIRST_TILE.index(x)
           for x in [("rows", NTG - 1)] + [("pick", k) for k in range(NPICK - NHOT, NPICK)])
assert NTG == ROUNDS + 1


def weight_runs():
    held = {}
    for n, block, column, count in [copied for step in PACKING for copied in step]:
        held.update({(p, block + k): (p % NF, (column + k) % NF) for p in range(n) for k in range(count)})
    where = {}
    for (p, block), (i, j) in sorted(held.items(), key=lambda x: x[1][0] > x[1][1]):
        if i != j:
            where.setdefault((min(i, j), max(i, j)), (p, block))
    assert len(where) == NF * (NF - 1) // 2
    left = {at: j * (j - 1) // 2 + i for (i, j), at in where.items()}
    out = []
    while left:
        found = []
        for (p, block), row in left.items():
            down = across = 1
            while left.get((p + down, block)) == row + down:
                down += 1
            while (block + across) % JS and left.get((p, block + across)) == row + across:
                across += 1
            found += [(row, down, p, block, False), (row, across, p, block, True)]
        row, count, p, block, across = max(found, key=lambda x: x[1])
        for k in range(count):
            del left[(p, block + k) if across else (p + k, block)]
        out.append((row, count, p, block, across))
    return out


def runs(features):
    out = []
    for k, f in enumerate(features):
        if f is None:
            continue
        if out and out[-1][1] + out[-1][2] == f and out[-1][0] + out[-1][2] == k:
            out[-1] = (out[-1][0], out[-1][1], out[-1][2] + 1)
        else:
            out.append((k, f, 1))
    return out


def orders(i):
    if isinstance(i, int) and i in (0, PAIRS - 1):
        return (FIRST_OF_LAST, SECOND_OF_LAST) if i else (FIRST_OF_ALL, SECOND_TILE)
    return FIRST_TILE, SECOND_TILE


def emb_count(i, h, kind, k):
    first, second = orders(i)
    n = len(first) + second.index((kind, k)) if h else first.index((kind, k))
    return BANKS * i + n + 1


def build(nc, dense_ctx, ids, tables, W1, b1, W2, b2, W3, out):
    ids_tiles = ids.rearrange("(p t) f -> p t f", t=TILES)
    ctx_tiles = dense_ctx.rearrange("(p t) c -> p t c", t=TILES)
    ids_rows = nc.dram_tensor("ids_rows", (NPICK, BATCH), F16, kind="Internal").ap()

    from contextlib import ExitStack
    stack = ExitStack()
    with stack:
        def sb(name, shape, dt=F32):
            return stack.enter_context(nc.sbuf_tensor(name, shape, dt))

        def ps(name, shape):
            return stack.enter_context(nc.psum_tensor(name, shape, F32))

        def sem(name):
            return stack.enter_context(nc.semaphore(name))

        ids_sb = [sb(f"ids_{h}", [P, NF], I32) for h in range(2)]
        ctx_sb = sb("ctx_sb", [P, 2, CTX])
        rows = [sb(f"rows_{h}", [P, len(GATHERED), D]) for h in range(2)]
        embT = sb("embT", [P, 2 * P, QUAD])
        dots = sb("dots", [P, JS, 2 * P])
        w1_sb = sb("w1_sb", [P, JS, H1])
        w2_sb = sb("w2_sb", [P, C1, H2])
        w3_sb = sb("w3_sb", [P, C2])
        b1_sb = sb("b1_sb", [P, C1])
        b2_sb = sb("b2_sb", [P, C2])
        h1_sb = sb("h1_sb", [P, C1, 2 * P])
        h2_sb = sb("h2_sb", [P, C2, 2 * P])
        y_sb = sb("y_sb", [P, TILES])
        ident = sb("ident", [P, P])
        ids_all = sb("ids_all", [P, TILES, NF], I32)
        ids_f32 = sb("ids_f32", [P, NPICK, TILES])
        ids_f16 = sb("ids_f16", [NPICK * TILES, P], F16)
        ids_bc = sb("ids_bc", [P, NPICK, 2 * P], F16)
        row_of_i32 = sb("row_of_i32", [P, VC], I32)
        row_of = sb("row_of", [P, VC])
        stage = [sb(f"stage_{n}", [P, VC * D]) for n in range(NPICK - 2)]
        late_rows = rows[1][:, :, :].rearrange("p f d -> p (f d)")
        table_f32 = [late_rows[:, 0:VC * D], late_rows[:, VC * D:2 * VC * D], *(x[:, :] for x in stage)]
        more_rows = [stage[h][:, 0:len(MORE) * D].rearrange("p (f d) -> p f d", d=D) for h in range(2)]
        parts = sb("parts", [P, NPICK, PARTS, VC * D], F32R)
        hot = sb("hot", [P, NHOT, VC, 2 * P], F32R)

        pE = [ps(f"pE_{n}", [P, TG, P]) for n in range(2)]
        pG = [ps(f"pG_{n}", [P, RG, P]) for n in range(2)]
        pM = [ps(f"pM_{n}", [P, 2, 2 * P]) for n in range(2)]
        pY = pM[0][:, 1, 0:2]
        pI = pM[0][:, 0, 0:P]

        w_loaded = sem("w_loaded")
        ids_all_loaded = sem("ids_all_loaded")
        ids_cast = sem("ids_cast")
        ids_turned = sem("ids_turned")
        ids_f16_made = sem("ids_f16_made")
        ids_rows_stored = sem("ids_rows_stored")
        ids_bc_loaded = sem("ids_bc_loaded")
        row_of_steps = sem("row_of_steps")
        table_loaded = [sem(f"table_loaded_{k}") for k in range(NPICK)]
        part_s = sem("part_s")
        part_v = sem("part_v")
        w1_zeroed = sem("w1_zeroed")
        ident_steps = sem("ident_steps")
        zeroed = sem("zeroed")
        ids_loaded = [sem(f"ids_loaded_{h}") for h in range(2)]
        ctx_loaded = sem("ctx_loaded")
        arrived = [[sem(f"arrived_{h}_{g}") for g in range(NTG)] for h in range(2)]
        more_arrived = [sem(f"more_arrived_{h}") for h in range(2)]
        rows_free = sem("rows_free")
        tiles_begun = sem("tiles_begun")
        hot_made = sem("hot_made")
        emb_ready = sem("emb_ready")
        emb_copied = sem("emb_copied")
        multiplied = sem("multiplied")
        packed_v = sem("packed_v")
        packed_s = sem("packed_s")
        dots_v = sem("dots_v")
        dots_s = sem("dots_s")
        h1_summed = sem("h1_summed")
        h1_v, h1_s = sem("h1_v"), sem("h1_s")
        h2_summed = sem("h2_summed")
        h2_v, h2_s = sem("h2_v"), sem("h2_s")
        y_summed = sem("y_summed")
        y_copied = sem("y_copied")
        stored = sem("stored")

        w1_runs = weight_runs()
        W_DMAS = len(w1_runs) + 1 + 4

        block = stack.enter_context(nc.Block())

        def load_ids_bc(eng, i):
            eng.dma_start(ids_bc[:, :, :], ids_rows[:, bass.ds(2 * P * i, 2 * P)].partition_broadcast(P))\
               .then_inc(ids_bc_loaded, 16)

        @block.sync
        def _(sp):
            def load_ids(h, i):
                sp.dma_start(ids_sb[h][:, :], ids_tiles[:, 2 * i + h, :]).then_inc(ids_loaded[h], 16)

            def load_ctx(i):
                sp.dma_start(ctx_sb[:, :, :], ctx_tiles[:, bass.ds(2 * i, 2), :]).then_inc(ctx_loaded, 16)

            def load_table(k):
                sp.dma_start(table_f32[k][0:VP, :], tables[PICKED[k]].rearrange("(p c) d -> p (c d)", c=VC))\
                  .then_inc(table_loaded[k], 16)

            load_ids(0, 0)
            sp.dma_start(ids_all[:, :, :], ids_tiles).then_inc(ids_all_loaded, 16)
            for k in range(3):
                load_table(k)
            sp.wait_ge(ids_f16_made, 1)
            sp.dma_start(ids_rows.rearrange("f (t p) -> (f t) p", p=P), ids_f16[:, :]).then_inc(ids_rows_stored, 16)
            load_table(3)
            sp.wait_ge(ids_rows_stored, 16)
            load_ids_bc(sp, 0)
            load_ids(1, 0)
            load_ctx(0)
            for k in range(4, NPICK):
                load_table(k)
            sp.wait_ge(w1_zeroed, 1)
            for row, count, place, b, across in w1_runs:
                p, s = QUAD * (b // JS) + place, b % JS
                to = w1_sb[p:p + 1, s:s + count, :] if across else w1_sb[p:p + count, s, :]
                rows_of_w1 = W1[row:row + count, :]
                sp.dma_start(to, rows_of_w1.unsqueeze(0) if across else rows_of_w1).then_inc(w_loaded, 16)
            sp.dma_start(w1_sb[CTX_ROW:CTX_ROW + CTX, CTX_BLOCK % JS, :], W1[NF * (NF - 1) // 2:, :])\
              .then_inc(w_loaded, 16)
            sp.dma_start(w2_sb[:, :, :], W2.rearrange("(c p) n -> p c n", p=P)).then_inc(w_loaded, 16)
            sp.dma_start(w3_sb[:, :], W3.rearrange("(c p) o -> p (c o)", p=P),
                         allow_slow_non_contiguous=True).then_inc(w_loaded, 16)
            sp.dma_start(b1_sb[:, :], b1.rearrange("(c p) -> p c", p=P),
                         allow_slow_non_contiguous=True).then_inc(w_loaded, 16)
            sp.dma_start(b2_sb[:, :], b2.rearrange("(c p) -> p c", p=P),
                         allow_slow_non_contiguous=True).then_inc(w_loaded, 16)
            with sp.Fori(1, PAIRS) as i:
                for h in range(2):
                    sp.wait_ge(emb_ready, emb_count(i - 1, h, "rows", NTG - 1))
                    load_ids(h, i)
                load_ctx(i)
            sp.wait_ge(y_copied, PAIRS + 2)
            sp.dma_start(out.rearrange("(p t) o -> p (t o)", t=TILES), y_sb[:, :]).then_inc(stored, 16)
            sp.wait_ge(stored, 16)

        @block.gpsimd
        def _(pool):
            def gather(to, f, h, done):
                pool.indirect_dma_start(to, None, tables[f], bass.IndirectOffsetOnAxis(ids_sb[h][:, f:f + 1], 0))\
                    .then_inc(done, 16)

            def gather_pair(i, first, last):
                for h in range(2):
                    if not first:
                        pool.wait_ge(emb_ready, emb_count(i - 1, h, "rows", NTG - 1))
                        pool.sem_inc(rows_free, 1)
                    if first and h == 1:
                        pool.wait_ge(part_v, 2)
                    pool.wait_ge(ids_loaded[h], 16 * i + 16)
                    pool.sem_inc(tiles_begun, 1)
                    for kind, g in orders(PAIRS - 1 if last else 1)[h]:
                        if kind == "more":
                            for n, f in enumerate(MORE):
                                gather(more_rows[h][:, n, :], f, h, more_arrived[h])
                        if kind == "rows":
                            for f in GROUPS[g]:
                                gather(rows[h][:, GATHERED.index(f), :], f, h, arrived[h][g])

            pool.memset(ident[:, :], 0.0).then_inc(ident_steps, 1)
            pool.iota(row_of_i32[:, :], [[1, VC]], base=0, channel_multiplier=VC).then_inc(row_of_steps, 1)
            pool.wait_ge(ident_steps, 1)
            pool.affine_select(out=ident[:, :], in_=ident[:, :], compare_op=ALU.not_equal, fill=1.0,
                               base=0, pattern=[[-1, P]], channel_multiplier=1).then_inc(ident_steps, 1)
            gather_pair(0, True, False)
            with pool.Fori(1, PAIRS - 1) as i:
                gather_pair(i, False, False)
            pool.wait_ge(part_v, NPICK)
            gather_pair(PAIRS - 1, False, True)

        @block.tensor
        def _(pe):
            def bank_free(n, i, first):
                if n >= 2 or not first:
                    pe.wait_ge(emb_copied, BANKS * i + n - 1)

            def transpose_group(h, g, n, i, first=False):
                pe.wait_ge(arrived[h][g], 16 * TG * (i + 1))
                bank_free(n, i, first)
                for k, f in enumerate(GROUPS[g]):
                    last = nc.tensor.transpose(pE[n % 2][:, k, :], rows[h][:, GATHERED.index(f), :], ident[:, :])
                last.then_inc(emb_ready, 1)

            def transpose_more(h, n, i):
                pe.wait_ge(more_arrived[h], 16 * len(MORE))
                bank_free(n, i, False)
                for k in range(len(MORE)):
                    last = nc.tensor.transpose(pE[n % 2][:, k, :], more_rows[h][:, k, :], ident[:, :])
                last.then_inc(emb_ready, 1)

            def transpose_contexts(n, i, first):
                pe.wait_ge(ctx_loaded, 16 * i + 16)
                bank_free(n, i, first)
                for h in range(2):
                    last = nc.tensor.transpose(pE[n % 2][0:CTX, h, :], ctx_sb[:, h, :], ident[:, :])
                last.then_inc(emb_ready, 1)

            def pick(k, n, i, first=False):
                if first:
                    pe.wait_ge(part_v, k + 1)
                pe.wait_ge(hot_made, NPICK * i + k + 1)
                bank_free(n, i, first)
                for c in range(VC):
                    for part in range(PARTS):
                        last = nc.tensor.matmul(
                            pE[n % 2][:, 0:2, :].rearrange("p a b -> p (a b)"), parts[0:VP, k, part, D * c:D * c + D],
                            hot[0:VP, k % NHOT, c, :], start=(c + part == 0), stop=(c == VC - 1 and part == PARTS - 1))
                last.then_inc(emb_ready, 1)

            def multiply_round(h, k, i, first=False):
                if k == 0:
                    first_tile_banks, second_tile_banks = map(len, orders(i))
                    pe.wait_ge(emb_copied, BANKS * i + first_tile_banks + h * second_tile_banks)
                if not (first and k < 2):
                    pe.wait_ge(dots_v, 2 * ROUNDS * i + ROUNDS * h + k - 1)
                    pe.wait_ge(dots_s, 2 * ROUNDS * i + ROUNDS * h + k - 1)
                for n in range(RG):
                    s = P * h + SG * (RG * k + n)
                    last = nc.tensor.matmul(
                        pG[k % 2][0:PROWS, n, 0:SG * NJ],
                        embT[:, s:s + SG, :].rearrange("p s f -> p (s f)")[:, 0:PROWS],
                        embT[:, s:s + SG, X:X + NJ], start=True, stop=True)
                last.then_inc(multiplied, 1)

            def layer1(n, rounds, at=0, size=2 * P, banks=(0, 1)):
                pe.wait_ge(dots_v, rounds)
                pe.wait_ge(dots_s, rounds)
                pe.wait_ge(y_copied, n + 1)
                for c in [2 * bank + k for bank in banks for k in range(2)]:
                    for s in range(JS):
                        last = nc.tensor.matmul(pM[c // 2][:, c % 2, 0:size], w1_sb[:, s, P * c:P * c + P],
                                                dots[:, s, at:at + size], start=(s == 0), stop=(s == JS - 1))
                    if c % 2:
                        last.then_inc(h1_summed, 1)

            def layer2(n, size=2 * P):
                pe.wait_ge(h1_s, 2 * n + 2)
                for c in range(C2):
                    for k in range(C1):
                        if c == 0 and k == 2:
                            pe.wait_ge(h1_v, 2 * n + 2)
                        last = nc.tensor.matmul(pM[c][:, 0, 0:size], w2_sb[:, k, P * c:P * c + P], h1_sb[:, k, 0:size],
                                                start=(k == 0), stop=(k == C1 - 1))
                    last.then_inc(h2_summed, 1)

            def layer3(n, size=2 * P):
                pe.wait_ge(h2_s, n + 1)
                pe.wait_ge(h2_v, n + 1)
                for h in range(size // P):
                    for k in range(C2):
                        last = nc.tensor.matmul(pY[:, h:h + 1], h2_sb[:, k, P * h:P * h + P],
                                                w3_sb[:, k:k + 1], start=(k == 0), stop=(k == C2 - 1))
                last.then_inc(y_summed, 1)

            def first_tile(i, first):
                for n, (kind, k) in enumerate(orders(i)[0]):
                    if kind == "more":
                        transpose_more(0, n, i)
                    elif kind == "rows":
                        transpose_group(0, k, n, i, first)
                        if not first and k < ROUNDS:
                            multiply_round(1, k, i - 1)
                    else:
                        pick(k, n, i, first)

            def second_tile(i, first):
                if not first:
                    layer1(i - 1, 2 * ROUNDS * i)
                for n, (kind, g) in enumerate(SECOND_TILE, len(FIRST_TILE)):
                    if kind == "contexts":
                        transpose_contexts(n, i, first)
                        continue
                    transpose_group(1, g, n, i, first)
                    if g == 2 and not first:
                        layer2(i - 1)
                    if g == 4 and not first:
                        layer3(i - 1)
                    if g != 2:
                        multiply_round(0, g - (g > 2), i, first)

            def last_tiles(i):
                layer1(i - 1, 2 * ROUNDS * i)
                n = len(FIRST_OF_LAST)
                transpose_more(1, n, i)
                transpose_group(1, 0, n + 1, i)
                multiply_round(0, 0, i)
                transpose_contexts(n + 2, i, False)
                transpose_group(1, 1, n + 3, i)
                multiply_round(0, 1, i)
                transpose_group(1, 2, n + 4, i)
                multiply_round(0, 2, i)
                multiply_round(0, 3, i)
                layer2(i - 1)
                transpose_group(1, 3, n + 5, i)
                layer3(i - 1)
                transpose_group(1, 4, n + 6, i)
                layer1(i, 2 * ROUNDS * i + ROUNDS, 0, P, (0,))
                multiply_round(1, 0, i)
                multiply_round(1, 1, i)
                layer1(i, 2 * ROUNDS * i + ROUNDS, 0, P, (1,))
                multiply_round(1, 2, i)
                multiply_round(1, 3, i)
                layer2(i, P)
                for k in range(10):
                    nc.tensor.transpose(pE[0][:, 0, :], ident[:, :], ident[:, :])
                layer3(i, P)
                layer1(i + 1, 2 * ROUNDS * (i + 1), P, P)
                layer2(i + 1, P)
                layer3(i + 1, P)

            pe.wait_ge(ident_steps, 2)
            pe.wait_ge(ids_cast, 1)
            nc.tensor.transpose(pI[0:NPICK * TILES, :], ids_f32[:, :, :].rearrange("p f t -> p (f t)"), ident[:, :])\
                .then_inc(ids_turned, 1)
            first_tile(0, True)
            pe.wait_ge(zeroed, 2)
            second_tile(0, True)
            pe.wait_ge(w_loaded, 16 * W_DMAS)
            with pe.Fori(1, PAIRS - 1) as i:
                first_tile(i, False)
                second_tile(i, False)
            first_tile(PAIRS - 1, False)
            last_tiles(PAIRS - 1)

        def quadrants(i, h, k, own):
            last = isinstance(i, int) and i == PAIRS - 1
            parted = (h, k) == (1, 2 if last else 3)
            return {"vector": (0,) if parted else (0, 1), "scalar": (1, 2, 3) if parted else (2, 3)}[own]

        def copy_dots(eng, copy, h, k, i, own, packed, done):
            rounds = [(tile, n) for tile in range(2) for n in range(ROUNDS)]
            of_pair = sum(len(quadrants(0, *x, own)) for x in rounds)
            copied = of_pair * i + sum(len(quadrants(i, *x, own)) for x in rounds[:ROUNDS * h + k])
            before = copied * (STEPS - 1)
            mine = quadrants(i, h, k, own)
            for step in range(STEPS):
                for at, q in enumerate(mine):
                    if step:
                        eng.wait_ge(packed, before + (step - 1) * len(mine) + at + 1)
                    s0 = P * h + SG * RG * k + q
                    for n, b, column, count in PACKING[step]:
                        r, slot, c = QUAD * (b // JS), b % JS, NJ * q + column - X
                        last = copy(
                            dots[r:r + n, slot:slot + count, s0:s0 + SG * RG - SG + 1:SG].rearrange("p j n -> p n j"),
                            pG[k % 2][QUAD * q:QUAD * q + n, :, c:c + count])
                    if step < STEPS - 1:
                        last.then_inc(packed, 1)
            last.then_inc(done, 1)

        def copy_embeddings(copy, bank, h, kind, k):
            if kind == "pick":
                f = PICKED[k]
                for place in (f, NF + f) if f < HUBS else (f,):
                    last = copy(embT[:, :, place], bank[:, 0:2, :].rearrange("p a b -> p (a b)"))
            elif kind == "contexts":
                last = copy(dots[CTX_ROW:CTX_ROW + CTX, CTX_BLOCK % JS, :],
                            bank[0:CTX, 0:2, :].rearrange("p a b -> p (a b)"))
            else:
                features = GROUPS[k] if kind == "rows" else MORE
                hubs = [f if f < HUBS else None for f in features]
                for at, f, count in runs(features) + [(at, NF + f, count) for at, f, count in runs(hubs)]:
                    last = copy(embT[:, P * h:P * h + P, f:f + count].rearrange("p s f -> p f s"),
                                bank[:, at:at + count, :])
            last.then_inc(emb_copied, 1)

        @block.vector
        def _(dve):
            def make_hot(k, i, first):
                if k >= NHOT:
                    dve.wait_ge(emb_ready, emb_count(i, 0, "pick", k - NHOT))
                elif not first:
                    dve.wait_ge(emb_ready, emb_count(i - 1, 0, "pick", k + NHOT * ((NPICK - 1 - k) // NHOT)))
                if k == 0:
                    dve.wait_ge(ids_bc_loaded, 16 * i + 16)
                for c in range(VC):
                    last = nc.vector.tensor_scalar(hot[0:VP, k % NHOT, c, :], ids_bc[0:VP, k, :],
                                                   row_of[0:VP, c:c + 1], None, ALU.is_equal)
                last.then_inc(hot_made, 1)

            def copy_round(h, k, i):
                dve.wait_ge(multiplied, 2 * ROUNDS * i + ROUNDS * h + k + 1)
                copy_dots(dve, nc.vector.tensor_copy, h, k, i, "vector", packed_v, dots_v)

            def relu1(n, size=2 * P):
                dve.wait_ge(h1_summed, 2 * n + 2)
                for c in (2, 3):
                    nc.vector.tensor_scalar(h1_sb[:, c, 0:size], pM[1][:, c % 2, 0:size], b1_sb[:, c:c + 1], 0.0,
                                            ALU.add, ALU.max).then_inc(h1_v, 1)

            def relu2(n, size=2 * P):
                dve.wait_ge(h2_summed, C2 * n + 2)
                nc.vector.tensor_scalar(h2_sb[:, 1, 0:size], pM[1][:, 0, 0:size], b2_sb[:, 1:2], 0.0,
                                        ALU.add, ALU.max).then_inc(h2_v, 1)

            def copy_y(n, at, size=2):
                dve.wait_ge(y_summed, n + 1)
                nc.vector.tensor_copy(y_sb[:, bass.ds(at, size)], pY[:, 0:size]).then_inc(y_copied, 1)

            def first_tile(i):
                for r in range(ROUNDS):
                    copy_round(1, r, i - 1)
                for kind, k in orders(i)[0]:
                    if kind == "pick" and k >= NHOT:
                        make_hot(k, i, False)

            def second_tile(i):
                make_hot(0, i + 1, False)
                relu1(i - 1)
                make_hot(1, i + 1, False)
                copy_round(0, 0, i)
                copy_round(0, 1, i)
                make_hot(2, i + 1, False)
                relu2(i - 1)
                copy_round(0, 2, i)
                copy_y(i - 1, 2 * (i - 1))
                copy_round(0, 3, i)

            def last_tiles(i):
                relu1(i - 1)
                for k in range(ROUNDS):
                    copy_round(0, k, i)
                relu2(i - 1)
                copy_y(i - 1, 2 * (i - 1))
                copy_round(1, 0, i)
                copy_round(1, 1, i)
                relu1(i, P)
                copy_round(1, 2, i)
                copy_round(1, 3, i)
                relu2(i, P)
                copy_y(i, TILES - 2, 1)
                relu1(i + 1, P)
                relu2(i + 1, P)
                copy_y(i + 1, TILES - 1, 1)

            def second_part(k):
                dve.wait_ge(part_s, k + 1)
                nc.vector.tensor_tensor(parts[0:VP, k, 1, :], table_f32[k][0:VP, :], parts[0:VP, k, 0, :],
                                        ALU.subtract).then_inc(part_v, 1)

            nc.vector.memset(w1_sb[:, :, :], 0.0).then_inc(w1_zeroed, 1)
            dve.wait_ge(ids_all_loaded, 16)
            for k, f in enumerate(PICKED):
                last = nc.vector.tensor_copy(ids_f32[:, k, :], ids_all[:, :, f])
            last.then_inc(ids_cast, 1)
            dve.wait_ge(row_of_steps, 1)
            nc.vector.tensor_copy(row_of[:, :], row_of_i32[:, :]).then_inc(row_of_steps, 1)
            for k in range(4):
                second_part(k)
            dve.wait_ge(row_of_steps, 2)
            for k in range(NPICK):
                make_hot(k, 0, True)
                if k + 4 < NPICK:
                    second_part(k + 4)
                if k == 3:
                    nc.vector.memset(embT[:, :, PLACES:QUAD], 0.0).then_inc(zeroed, 1)
                if k == 4:
                    nc.vector.memset(dots[:, :, :], 0.0).then_inc(zeroed, 1)
            nc.vector.memset(y_sb[:, :], 0.0).then_inc(y_copied, 1)
            dve.wait_ge(zeroed, 2)
            for k in range(NHOT):
                make_hot(k, 1, False)
            for r in range(ROUNDS):
                copy_round(0, r, 0)
            dve.wait_ge(w_loaded, 16 * W_DMAS)
            with dve.Fori(1, PAIRS - 1) as i:
                first_tile(i)
                second_tile(i)
            first_tile(PAIRS - 1)
            last_tiles(PAIRS - 1)

        @block.scalar
        def _(act):
            def copy_bank(h, n, kind, k, i):
                act.wait_ge(emb_ready, BANKS * i + n + 1)
                copy_embeddings(nc.scalar.copy, pE[n % 2], h, kind, k)

            def copy_round(h, k, i):
                act.wait_ge(multiplied, 2 * ROUNDS * i + ROUNDS * h + k + 1)
                copy_dots(act, nc.scalar.copy, h, k, i, "scalar", packed_s, dots_s)

            def relu1(n, size=2 * P):
                act.wait_ge(h1_summed, 2 * n + 1)
                for c in (0, 1):
                    nc.scalar.activation(h1_sb[:, c, 0:size], pM[0][:, c, 0:size], ACT.Relu, bias=b1_sb[:, c:c + 1])\
                        .then_inc(h1_s, 1)

            def relu2(n, size=2 * P):
                act.wait_ge(h2_summed, C2 * n + 1)
                nc.scalar.activation(h2_sb[:, 0, 0:size], pM[0][:, 0, 0:size], ACT.Relu, bias=b2_sb[:, 0:1])\
                    .then_inc(h2_s, 1)

            def first_tile(i, first):
                for n, (kind, k) in enumerate(orders(i)[0]):
                    if (kind, k) == ("pick", NPICK - 1):
                        act.wait_ge(hot_made, NPICK * i + NPICK)
                        load_ids_bc(act, i + 1)
                    copy_bank(0, n, kind, k, i)
                    if kind == "rows" and not first and k < ROUNDS:
                        copy_round(1, k, i - 1)

            def second_tile(i, first):
                if not first:
                    relu1(i - 1)
                for n, (kind, g) in enumerate(SECOND_TILE, len(FIRST_TILE)):
                    copy_bank(1, n, kind, g, i)
                    if kind == "contexts":
                        continue
                    if g == 2 and not first:
                        relu2(i - 1)
                    if g != 2:
                        copy_round(0, g - (g > 2), i)

            def last_tiles(i):
                relu1(i - 1)
                n = len(FIRST_OF_LAST)
                copy_bank(1, n, "more", 0, i)
                copy_bank(1, n + 1, "rows", 0, i)
                copy_round(0, 0, i)
                copy_bank(1, n + 2, "contexts", 0, i)
                copy_bank(1, n + 3, "rows", 1, i)
                copy_round(0, 1, i)
                copy_bank(1, n + 4, "rows", 2, i)
                copy_round(0, 2, i)
                copy_round(0, 3, i)
                relu2(i - 1)
                copy_bank(1, n + 5, "rows", 3, i)
                copy_bank(1, n + 6, "rows", 4, i)
                relu1(i, P)
                for k in range(ROUNDS):
                    copy_round(1, k, i)
                relu2(i, P)
                relu1(i + 1, P)
                relu2(i + 1, P)

            act.wait_ge(ids_turned, 1)
            nc.scalar.copy(ids_f16[:, :], pI[0:NPICK * TILES, :]).then_inc(ids_f16_made, 1)
            for k in range(NPICK):
                act.wait_ge(table_loaded[k], 16)
                nc.scalar.copy(parts[0:VP, k, 0, :], table_f32[k][0:VP, :]).then_inc(part_s, 1)
            first_tile(0, True)
            act.wait_ge(zeroed, 2)
            second_tile(0, True)
            act.wait_ge(w_loaded, 16 * W_DMAS)
            with act.Fori(1, PAIRS - 1) as i:
                first_tile(i, False)
                second_tile(i, False)
            first_tile(PAIRS - 1, False)
            last_tiles(PAIRS - 1)


_TABLES = [f"tbl_{f}" for f in range(NF)]
_INS = ["dense_ctx", "ids", *_TABLES, "W_top1", "b_top1", "W_top2", "b_top2", "W_top3"]


def kernel(**inputs):
    import numpy as _np
    import concourse.bacc as _bacc
    from concourse import mybir as _mybir
    from concourse.bass_utils import run_bass_kernel_spmd as _run

    nc = _bacc.Bacc("TRN2", target_bir_lowering=False, num_devices=1)
    arrays, aps = {}, {}
    for name in _INS:
        a = _np.ascontiguousarray(inputs[name])
        arrays[f"in_{name}_dram"] = a
        aps[name] = nc.dram_tensor(f"in_{name}_dram", a.shape, _mybir.dt.from_np(a.dtype), kind="ExternalInput").ap()
    out = nc.dram_tensor("out_0_dram", (BATCH, 1), _mybir.dt.float32, kind="ExternalOutput").ap()
    build(nc, aps["dense_ctx"], aps["ids"], [aps[t] for t in _TABLES], aps["W_top1"], aps["b_top1"],
          aps["W_top2"], aps["b_top2"], aps["W_top3"], out)
    r = _run(nc, [arrays], core_ids=[0])
    return r.results[0]["out_0_dram"]
```
